# Optimizing a Trainium2 kernel written in Bass

```python
import numpy as np
import jax
import jax.numpy as jnp

def _softmax(x, axis=-1):
    return jax.nn.softmax(x, axis=axis)
def _gelu(x):
    return jax.nn.gelu(x, approximate=True)
def _silu(x):
    return jax.nn.silu(x)
def _sigmoid(x):
    return jax.nn.sigmoid(x)
def _layernorm(x, axis=-1, eps=1e-5):
    m = jnp.mean(x, axis=axis, keepdims=True)
    v = jnp.var(x, axis=axis, keepdims=True)
    return (x - m) / jnp.sqrt(v + eps)
def _scatter_add(tgt, idx, src, axis=0):
    return tgt.at[idx].add(src)
def _segment_sum(src, seg, n):
    return jax.ops.segment_sum(src, seg, n)

kernel_name = 'mk_adj_preln_d1_adj_256_2d266e'

def setup_inputs(seed: int = 0):
    np.random.seed(seed)
    _w = jnp.asarray
    def _rec_inputs():
        import jax
        import jax.numpy as jnp
        _gk = jax.random.key(seed)
        x = -0.0002928 + 1 * jax.random.normal(jax.random.fold_in(_gk, 1), (32, 512, 256), jnp.float32)
        _w = (1.0 + jnp.arange(512, dtype=jnp.float32)) ** -0.5
        _w = _w / _w.mean()
        _pij = jnp.clip(0.0078125 * _w[:, None] * _w[None, :], 0.0, 1.0)
        _a = jax.random.uniform(jax.random.fold_in(_gk, 2), (32, 512, 512)) < _pij
        adj = _a.astype(jnp.int32)
        return x, adj
    x, adj = _rec_inputs()
    def _L0_gnn_setup():
        import jax, jax.numpy as jnp
        import numpy as np
        OUT = 256
        NUM_LAYERS = 3

        def _gru_cell(inp, h, w_ih, w_hh, b_ih, b_hh):
            gi = inp @ w_ih.T + b_ih
            gh = h @ w_hh.T + b_hh
            i_r, i_z, i_n = jnp.split(gi, 3, axis=-1)
            h_r, h_z, h_n = jnp.split(gh, 3, axis=-1)
            r = jax.nn.sigmoid(i_r + h_r)
            z = jax.nn.sigmoid(i_z + h_z)
            n = jnp.tanh(i_n + r * h_n)
            return (1.0 - z) * n + z * h
        key = jax.random.key(seed)
        ks = jax.random.split(key, 8)
        B, N, D = (32, 512, 256)
        x = jax.random.normal(ks[0], (B, N, D), dtype=jnp.float32)
        adj = jax.random.randint(ks[1], (B, N, N), 0, 2, dtype=jnp.int32)
        s = 1.0 / np.sqrt(OUT)
        weight = jax.random.uniform(ks[2], (NUM_LAYERS, OUT, OUT), jnp.float32, -s, s)
        w_ih = jax.random.uniform(ks[3], (3 * OUT, OUT), jnp.float32, -s, s)
        w_hh = jax.random.uniform(ks[4], (3 * OUT, OUT), jnp.float32, -s, s)
        b_ih = jax.random.uniform(ks[5], (3 * OUT,), jnp.float32, -s, s)
        b_hh = jax.random.uniform(ks[6], (3 * OUT,), jnp.float32, -s, s)
        return {'x': x, 'adj': adj, 'weight': weight, 'w_ih': w_ih, 'w_hh': w_hh, 'b_ih': b_ih, 'b_hh': b_hh}
    _L0_gnn_all = _L0_gnn_setup()
    _L0_gnn_in = {k: v for k, v in _L0_gnn_all.items() if k in ('weight', 'w_ih', 'w_hh', 'b_ih', 'b_hh', )}
    del _L0_gnn_all

    return {
        "x": x,
        "adj": adj,
        "L0_gnn_weight": _L0_gnn_in["weight"],
        "L0_gnn_w_ih": _L0_gnn_in["w_ih"],
        "L0_gnn_w_hh": _L0_gnn_in["w_hh"],
        "L0_gnn_b_ih": _L0_gnn_in["b_ih"],
        "L0_gnn_b_hh": _L0_gnn_in["b_hh"],
    }

def reference(x, adj, L0_gnn_weight, L0_gnn_w_ih, L0_gnn_w_hh, L0_gnn_b_ih, L0_gnn_b_hh):
    import jax
    import jax.numpy as jnp
    def _L0_gnn_ref(x, adj, weight, w_ih, w_hh, b_ih, b_hh):
        import jax, jax.numpy as jnp
        import numpy as np
        OUT = 256
        NUM_LAYERS = 3

        def _gru_cell(inp, h, w_ih, w_hh, b_ih, b_hh):
            gi = inp @ w_ih.T + b_ih
            gh = h @ w_hh.T + b_hh
            i_r, i_z, i_n = jnp.split(gi, 3, axis=-1)
            h_r, h_z, h_n = jnp.split(gh, 3, axis=-1)
            r = jax.nn.sigmoid(i_r + h_r)
            z = jax.nn.sigmoid(i_z + h_z)
            n = jnp.tanh(i_n + r * h_n)
            return (1.0 - z) * n + z * h
        A = (adj != 0).astype(x.dtype)
        h = x
        L = weight.shape[0]
        for i in range(L):
            m = jnp.einsum('bnd,de->bne', h, weight[i])
            aggr = jnp.einsum('bst,bsd->btd', A, m)
            h = _gru_cell(aggr, h, w_ih, w_hh, b_ih, b_hh)
        return h

    h = jnp.maximum(_layernorm(x, axis=-1), 0.0)
    x = x + _L0_gnn_ref(h, adj, L0_gnn_weight, L0_gnn_w_ih, L0_gnn_w_hh, L0_gnn_b_ih, L0_gnn_b_hh)
    return x


_drawn_inputs = setup_inputs


def setup_inputs(seed=0):
    import zlib

    import numpy as np

    out = dict(_drawn_inputs(seed))
    spreads = {}
    factors = {'L0_gnn_b_hh': 3.304}
    for name, (base, spread) in spreads.items():
        noise = np.random.default_rng([zlib.crc32(name.encode()), seed]).standard_normal(out[name].shape)
        drawn = base * np.exp(spread * noise) if base else spread * noise
        out[name] = jnp.asarray(drawn.astype(out[name].dtype))
    for name, factor in factors.items():
        out[name] = (out[name] * factor).astype(out[name].dtype)
    return out
```

```python
from contextlib import ExitStack

import concourse.bass as bass
from concourse import mybir

F32 = mybir.dt.float32
F16 = mybir.dt.float16
I32 = mybir.dt.int32
ALU = mybir.AluOpType
ACT = mybir.ActivationFunctionType
AX = mybir.AxisListType

P = 128
H_SCALE = 2.0 ** 11
AGG_SCALE = 2.0 ** 2
LN_EPS = 1e-5
POW2_BITS = 0x7F800000


def gnn_kernel(nc, x, adj, w_t, wih_t, whh_t, bih, bhh, out):
    B, N, D = x.shape
    LAYERS = w_t.shape[0]
    GATES = wih_t.shape[1]
    SC = N // P
    DC = D // P
    GC = GATES // P
    PAIRS = B // 2
    ITEMS = 2 * LAYERS
    SPLITS = ITEMS - 2
    WCOLS = GATES // 2
    WPRODS = LAYERS * DC * 2

    ctx = ExitStack()
    with ctx:
        def sb(name, shape, dt):
            return ctx.enter_context(nc.sbuf_tensor(name, shape, dt))

        def bank(name, shape, dt):
            return ctx.enter_context(nc.psum_tensor(name, shape, dt))

        def sem(name):
            return ctx.enter_context(nc.semaphore(name))

        w_sb = sb("w_sb", [P, LAYERS, DC, D], F32)
        wih_sb = sb("wih_sb", [P, DC, GATES], F32)
        whh_sb = sb("whh_sb", [P, DC, GATES], F32)
        wx_hi = sb("wx_hi", [P, LAYERS, DC, GATES], F16)
        wx_lo = sb("wx_lo", [P, LAYERS, DC, GATES], F16)
        wh_hi = sb("wh_hi", [P, DC, GATES], F16)
        wh_lo = sb("wh_lo", [P, DC, GATES], F16)
        bih_sb = sb("bih_sb", [P, GC], F32)
        bhh_sb = sb("bhh_sb", [P, GC], F32)
        bsum = sb("bsum", [P, GC], F32)
        bhn = sb("bhn", [P, DC], F32)
        ident_h = sb("ident_h", [P, P], F16)
        ident_f = sb("ident_f", [P, P], F32)
        minus_half = sb("minus_half", [P, SC], F32)
        wmax = sb("wmax", [P, 3], F32)
        wmax_all = sb("wmax_all", [P, 3], F32)
        bound = sb("bound", [P, 2], F32)
        pow2 = sb("pow2", [P, 1], F32)
        rpow2 = sb("rpow2", [P, 1], F32)
        gate_unscale = sb("gate_unscale", [P, 1], F32)
        gate_scale = sb("gate_scale", [P, 1], F32)
        wx_scale = sb("wx_scale", [P, 1], F32)
        wh_scale = sb("wh_scale", [P, 1], F32)

        adj_in = [sb(f"adj_in{m}", [P, SC, N], I32) for m in range(2)]
        mask = [sb(f"mask{m}", [P, SC, N], F16) for m in range(2)]
        x_in = [sb(f"x_in{m}", [P, SC, D], F32) for m in range(2)]
        x_out = [sb(f"x_out{m}", [P, SC, D], F32) for m in range(2)]
        nat_hi = [sb(f"nat_hi{m}", [P, SC, D], F16) for m in range(2)]
        nat_lo = [sb(f"nat_lo{m}", [P, SC, D], F16) for m in range(2)]
        hT_hi = [[sb(f"hT_hi{m}_{s}", [P, DC, N], F16) for s in range(2)] for m in range(2)]
        hT_lo = [[sb(f"hT_lo{m}_{s}", [P, DC, N], F16) for s in range(2)] for m in range(2)]
        hT = [sb(f"hT{m}", [P, DC, N], F32) for m in range(2)]
        ln_st = [sb(f"ln_st{m}", [P, SC, 6], F32) for m in range(2)]
        ln_mv = [sb(f"ln_mv{m}", [P, SC, 2], F32) for m in range(2)]
        ln_ve = [sb(f"ln_ve{m}", [P, SC], F32) for m in range(2)]
        ln_rstd = [sb(f"ln_rstd{m}", [P, SC], F32) for m in range(2)]
        ln_rs = [sb(f"ln_rs{m}", [P, SC], F32) for m in range(2)]
        ln_y = [sb(f"ln_y{m}", [P, SC, D], F32) for m in range(2)]

        agg_hi = sb("agg_hi", [P, DC, N], F16)
        agg_lo = sb("agg_lo", [P, DC, N], F16)
        r_sb = sb("r_sb", [P, DC, N], F32)
        z_sb = sb("z_sb", [P, DC, N], F32)
        n_sb = sb("n_sb", [P, DC, N], F32)
        pre_sb = sb("pre_sb", [P, DC, N], F32)
        dif_sb = sb("dif_sb", [P, DC, N], F32)

        agg_ps = [bank(f"agg_ps{j}", [P, N], F32) for j in range(DC)]
        r_ps = bank("r_ps", [P, N], F32)
        z_ps = bank("z_ps", [P, N], F32)
        in_ps = bank("in_ps", [P, N], F32)
        hn_ps = bank("hn_ps", [P, N], F32)
        turn_ps = [bank(f"turn_ps{i}", [P, 512], F32) for i in range(2)]
        turn_h = [t[:, :].bitcast(F16) for t in turn_ps]
        prod_ps = [r_ps, z_ps, in_ps, hn_ps]

        w_loaded = sem("w_loaded")
        whh_loaded = sem("whh_loaded")
        b_loaded = sem("b_loaded")
        consts_cleared = sem("consts_cleared")
        consts_ready = sem("consts_ready")
        wmax_ready = sem("wmax_ready")
        wmax_all_ready = sem("wmax_all_ready")
        scale_step = sem("scale_step")
        scales_ready = sem("scales_ready")
        biases_ready = sem("biases_ready")
        prod_ready = sem("prod_ready")
        prod_hi_ready = sem("prod_hi_ready")
        prod_lo_ready = sem("prod_lo_ready")
        wh_hi_ready = sem("wh_hi_ready")
        wh_lo_ready = sem("wh_lo_ready")
        x_loaded = [sem(f"x_loaded{m}") for m in range(2)]
        adj_loaded = [sem(f"adj_loaded{m}") for m in range(2)]
        stored = [sem(f"stored{m}") for m in range(2)]
        x_copied = sem("x_copied")
        mask_ready = sem("mask_ready")
        ln_stats = sem("ln_stats")
        ln_aggr = sem("ln_aggr")
        ln_eps_added = sem("ln_eps_added")
        ln_rstd_ready = sem("ln_rstd_ready")
        ln_rs_ready = sem("ln_rs_ready")
        ln_centered = sem("ln_centered")
        ln_hi_ready = sem("ln_hi_ready")
        ln_lo_ready = sem("ln_lo_ready")
        h0_summed = sem("h0_summed")
        out_turned = sem("out_turned")
        out_added = sem("out_added")
        turned_hi = sem("turned_hi")
        turned_lo = sem("turned_lo")
        turned_hi_copied = sem("turned_hi_copied")
        turned_lo_copied = sem("turned_lo_copied")
        agg_ready = sem("agg_ready")
        r_ready = sem("r_ready")
        z_ready = sem("z_ready")
        in_ready = sem("in_ready")
        hn_ready = sem("hn_ready")
        agg_hi_ready = sem("agg_hi_ready")
        agg_lo_ready = sem("agg_lo_ready")
        r_sig = sem("r_sig")
        z_sig = sem("z_sig")
        n_tanh = sem("n_tanh")
        gated = sem("gated")
        pre_ready = sem("pre_ready")
        dif_ready = sem("dif_ready")
        zdif_ready = sem("zdif_ready")
        h_new = sem("h_new")
        h_hi_ready = sem("h_hi_ready")
        h_lo_ready = sem("h_lo_ready")

        def graphs(p, m):
            return 2 * p + (m + 1)

        def loads(p):
            return 16 * p + 16

        def items(p, q):
            return ITEMS * p + (q + 1)

        def halves(p, q, j):
            return DC * ITEMS * p + (DC * q + j + 1)

        def splits(p, q, j):
            return DC * SPLITS * p + (DC * q + j + 1)

        block = ctx.enter_context(nc.Block())

        @block.sync
        def _(sp):
            def graph(t, p, m):
                return t[bass.ds(2 * p + m, 1)].rearrange("b (c p) f -> (b p) c f", p=P)

            def load_adj(p, m):
                sp.dma_start(adj_in[m][:, :, :], graph(adj, p, m)).then_inc(adj_loaded[m], 16)

            def load_x(p, m):
                sp.dma_start(x_in[m][:, :, :], graph(x, p, m)).then_inc(x_loaded[m], 16)

            def store(p, m):
                sp.wait_ge(out_added, 2 * graphs(p, m))
                sp.dma_start(graph(out, p, m), x_out[m][:, :, :]).then_inc(stored[m], 16)

            def pair(p, first=False, last=False):
                if not last:
                    for m in range(2):
                        sp.wait_ge(mask_ready, graphs(p, m))
                        load_adj(p + 1, m)
                if not first:
                    for m in range(2):
                        store(p - 1, m)
                if not last:
                    for m in range(2):
                        sp.wait_ge(x_copied, graphs(p, m))
                        load_x(p + 1, m)

            sp.dma_start(w_sb[:, :, :, :], w_t.rearrange("l (c p) d -> p l c d", p=P)).then_inc(w_loaded, 16)
            sp.dma_start(wih_sb[:, :, :], wih_t.rearrange("(c p) g -> p c g", p=P)).then_inc(w_loaded, 16)
            load_x(0, 0)
            sp.dma_start(whh_sb[:, :, :], whh_t.rearrange("(c p) g -> p c g", p=P)).then_inc(whh_loaded, 16)
            load_adj(0, 0)
            sp.dma_start(bih_sb[:, :], bih).then_inc(b_loaded, 16)
            sp.dma_start(bhh_sb[:, :], bhh).then_inc(b_loaded, 16)
            load_x(0, 1)
            load_adj(0, 1)
            pair(0, first=True)
            with sp.Fori(1, PAIRS - 1) as p:
                pair(p)
            pair(PAIRS - 1, last=True)
            for m in range(2):
                store(PAIRS - 1, m)
            for m in range(2):
                sp.wait_ge(stored[m], loads(PAIRS - 1))

        @block.gpsimd
        def _(pool):
            pool.memset(ident_h[:, :], 0.0).then_inc(consts_cleared, 1)
            pool.memset(ident_f[:, :], 0.0).then_inc(consts_cleared, 1)
            pool.memset(minus_half[:, :], -0.5).then_inc(consts_cleared, 1)
            pool.wait_ge(consts_cleared, 3)
            for t in (ident_h, ident_f):
                pool.affine_select(out=t[:, :], in_=t[:, :], compare_op=ALU.not_equal, fill=1.0, base=0,
                                   pattern=[[-1, P]], channel_multiplier=1).then_inc(consts_ready, 1)

            def rstd(p, m):
                pool.wait_ge(ln_eps_added, graphs(p, m))
                pool.tensor_tensor(ln_rstd[m][:, :], ln_ve[m][:, :], minus_half[:, :],
                                   ALU.pow).then_inc(ln_rstd_ready, 1)

            rstd(0, 0)
            pool.wait_ge(wmax_ready, 3)
            pool.partition_all_reduce(wmax_all[:, :], wmax[:, :], P,
                                      bass.bass_isa.ReduceOp.max).then_inc(wmax_all_ready, 1)
            rstd(0, 1)
            rstd(1, 0)
            rstd(1, 1)
            with pool.Fori(1, PAIRS - 1) as p:
                for m in range(2):
                    rstd(p + 1, m)

        @block.scalar
        def _(act):
            def ln_hi(m):
                act.activation(nat_hi[m][:, :, :], ln_y[m][:, :, :], ACT.Relu).then_inc(ln_hi_ready, 1)

            def copy_turned_hi(l, m):
                dst = hT_hi[m][0] if l == 0 else nat_hi[m]
                act.activation(dst[:, :, :].rearrange("p a b -> p (a b)"), turn_h[0],
                               ACT.Copy).then_inc(turned_hi_copied, 1)

            def copy_x(p, m, first):
                act.wait_ge(x_loaded[m], loads(p))
                if not first:
                    act.wait_ge(stored[m], loads(p - 1))
                act.activation(x_out[m][:, :, :], x_in[m][:, :, :], ACT.Copy).then_inc(x_copied, 1)

            def gates(p, q, j):
                l, m = q // 2, q % 2
                act.wait_ge(r_ready, halves(p, q, j))
                act.activation(r_sb[:, j, :], r_ps[:, :], ACT.Sigmoid, bias=bsum[:, j:j + 1],
                               scale=gate_unscale[:, 0:1]).then_inc(r_sig, 1)
                act.wait_ge(pre_ready, halves(p, q, j))
                act.activation(n_sb[:, j, :], pre_sb[:, j, :], ACT.Tanh, bias=bih_sb[:, 2 * DC + j:2 * DC + j + 1],
                               scale=gate_unscale[:, 0:1]).then_inc(n_tanh, 1)
                act.wait_ge(z_ready, halves(p, q, j))
                act.activation(z_sb[:, j, :], z_ps[:, :], ACT.Sigmoid, bias=bsum[:, DC + j:DC + j + 1],
                               scale=gate_unscale[:, 0:1]).then_inc(z_sig, 1)
                if l < LAYERS - 1:
                    act.wait_ge(h_new, halves(p, q, j))
                    act.activation(hT_hi[m][(l + 1) % 2][:, j, :], hT[m][:, j, :], ACT.Copy,
                                   scale=H_SCALE).then_inc(h_hi_ready, 1)

            def item(p, q, first, last):
                m = q % 2
                for j in range(DC):
                    act.wait_ge(agg_ready, halves(p, q, j))
                    act.activation(agg_hi[:, j, :], agg_ps[j][:, :], ACT.Copy,
                                   scale=AGG_SCALE / H_SCALE).then_inc(agg_hi_ready, 1)
                if 2 <= q < 4:
                    copy_x(p, m, first)
                gates(p, q, 0)
                if q < ITEMS - 1 or not last:
                    act.wait_ge(turned_hi, items(p, q + 1))
                    copy_turned_hi((q + 1) % ITEMS // 2, (q + 1) % 2)
                gates(p, q, 1)
                if q >= ITEMS - 2 and not last:
                    act.wait_ge(ln_centered, graphs(p + 1, m))
                    ln_hi(m)

            def pair(p, first=False, last=False):
                for q in range(ITEMS):
                    item(p, q, first, last)

            for m in range(2):
                act.wait_ge(ln_centered, graphs(0, m))
                ln_hi(m)
                if m == 0:
                    act.wait_ge(scales_ready, 4)
                    act.wait_ge(whh_loaded, 16)
                    act.activation(wh_hi[:, :, :], whh_sb[:, :, :], ACT.Copy,
                                   scale=wh_scale[:, 0:1]).then_inc(wh_hi_ready, 1)
                    for n in range(WPRODS):
                        l, c, g = n // (2 * DC), n // 2 % DC, n % 2
                        act.wait_ge(prod_ready, n + 1)
                        act.activation(wx_hi[:, l, c, g * WCOLS:(g + 1) * WCOLS], prod_ps[n % 4][:, 0:WCOLS],
                                       ACT.Copy, scale=wx_scale[:, 0:1]).then_inc(prod_hi_ready, 1)
                    act.wait_ge(turned_hi, 1)
                    copy_turned_hi(0, 0)
                    act.wait_ge(biases_ready, 2)
            pair(0, first=True)
            with act.Fori(1, PAIRS - 1) as p:
                pair(p)
            pair(PAIRS - 1, last=True)

        @block.vector
        def _(dve):
            def ln_statistics(m):
                for c in range(SC):
                    dve.bn_stats(ln_st[m][:, c, :], x_in[m][:, c, :]).then_inc(ln_stats, 1)

            def ln_mean_var(m):
                for c in range(SC):
                    dve.bn_aggr(ln_mv[m][:, c, :], ln_st[m][:, c, :]).then_inc(ln_aggr, 1)

            def ln_eps(m):
                dve.tensor_scalar(ln_ve[m][:, :], ln_mv[m][:, :, 1], LN_EPS, None, ALU.add).then_inc(ln_eps_added, 1)

            def ln_scale(m):
                dve.tensor_scalar(ln_rs[m][:, :], ln_rstd[m][:, :], H_SCALE, None, ALU.mult).then_inc(ln_rs_ready, 1)

            def ln_center(m):
                for c in range(SC):
                    last = dve.tensor_scalar(ln_y[m][:, c, :], x_in[m][:, c, :], ln_mv[m][:, c, 0:1],
                                             ln_rs[m][:, c:c + 1], ALU.subtract, ALU.mult)
                last.then_inc(ln_centered, 1)

            def ln_lo(m):
                dve.scalar_tensor_tensor(out=nat_lo[m][:, :, :], in0=ln_y[m][:, :, :], scalar=0.0,
                                         in1=nat_hi[m][:, :, :], op0=ALU.max, op1=ALU.subtract).then_inc(ln_lo_ready, 1)

            def make_mask(m):
                dve.tensor_scalar(mask[m][:, :, :], adj_in[m][:, :, :], 0.0, None,
                                  ALU.not_equal).then_inc(mask_ready, 1)

            def copy_turned_lo(p, q):
                l, m = q % ITEMS // 2, q % 2
                dst = hT_lo[m][0] if l == 0 else nat_lo[m]
                dve.wait_ge(turned_lo, items(p, q))
                dve.tensor_copy(dst[:, :, :].rearrange("p a b -> p (a b)"), turn_h[1]).then_inc(turned_lo_copied, 1)

            def sum_h0(p, m):
                dve.wait_ge(turned_hi_copied, items(p, m))
                dve.wait_ge(turned_lo_copied, items(p, m))
                dve.tensor_tensor(hT[m][:, :, :], hT_hi[m][0][:, :, :], hT_lo[m][0][:, :, :],
                                  ALU.add).then_inc(h0_summed, 1)

            def add_out(p, m):
                for i in range(2):
                    dve.wait_ge(out_turned, 2 * graphs(p, m) + (i - 1))
                    part = x_out[m][:, i * SC // 2:(i + 1) * SC // 2, :].rearrange("p c f -> p (c f)")
                    dve.tensor_tensor(part, turn_ps[i][:, :], part, ALU.add).then_inc(out_added, 1)

            def pre_n(p, q, j):
                dve.wait_ge(r_sig, halves(p, q, j))
                dve.wait_ge(hn_ready, halves(p, q, j))
                dve.scalar_tensor_tensor(out=pre_sb[:, j, :], in0=hn_ps[:, :], scalar=bhn[:, j:j + 1],
                                         in1=r_sb[:, j, :], op0=ALU.add, op1=ALU.mult).then_inc(gated, 1)
                dve.wait_ge(in_ready, halves(p, q, j))
                dve.wait_ge(gated, halves(p, q, j))
                dve.tensor_tensor(pre_sb[:, j, :], in_ps[:, :], pre_sb[:, j, :], ALU.add).then_inc(pre_ready, 1)

            def update(p, q, j):
                l, m = q // 2, q % 2
                dve.wait_ge(n_tanh, halves(p, q, j))
                if l == 0:
                    dve.wait_ge(h0_summed, graphs(p, m))
                    dve.scalar_tensor_tensor(out=dif_sb[:, j, :], in0=hT[m][:, j, :], scalar=1.0 / H_SCALE,
                                             in1=n_sb[:, j, :], op0=ALU.mult, op1=ALU.subtract).then_inc(dif_ready, 1)
                else:
                    dve.tensor_tensor(dif_sb[:, j, :], hT[m][:, j, :], n_sb[:, j, :],
                                      ALU.subtract).then_inc(dif_ready, 1)
                dve.wait_ge(z_sig, halves(p, q, j))
                dve.wait_ge(dif_ready, halves(p, q, j))
                dve.tensor_tensor(dif_sb[:, j, :], z_sb[:, j, :], dif_sb[:, j, :], ALU.mult).then_inc(zdif_ready, 1)
                dve.wait_ge(zdif_ready, halves(p, q, j))
                dve.tensor_tensor(hT[m][:, j, :], n_sb[:, j, :], dif_sb[:, j, :], ALU.add).then_inc(h_new, 1)

            def update_lo(p, q, j):
                l, m = q // 2, q % 2
                dve.wait_ge(h_hi_ready, splits(p, q, j))
                dve.scalar_tensor_tensor(out=hT_lo[m][(l + 1) % 2][:, j, :], in0=hT[m][:, j, :], scalar=H_SCALE,
                                         in1=hT_hi[m][(l + 1) % 2][:, j, :], op0=ALU.mult,
                                         op1=ALU.subtract).then_inc(h_lo_ready, 1)

            def item(p, q, first, last):
                l, m = q // 2, q % 2
                ahead = q >= ITEMS - 2 and not last
                for j in range(DC):
                    dve.wait_ge(agg_hi_ready, halves(p, q, j))
                    dve.scalar_tensor_tensor(out=agg_lo[:, j, :], in0=agg_ps[j][:, :], scalar=AGG_SCALE / H_SCALE,
                                             in1=agg_hi[:, j, :], op0=ALU.mult,
                                             op1=ALU.subtract).then_inc(agg_lo_ready, 1)
                if q < 2 and not first:
                    add_out(p - 1, m)
                if l == 0:
                    sum_h0(p, m)
                if ahead:
                    dve.wait_ge(x_loaded[m], loads(p + 1))
                    ln_statistics(m)
                pre_n(p, q, 0)
                if ahead:
                    dve.wait_ge(ln_stats, SC * graphs(p + 1, m))
                update(p, q, 0)
                if l < LAYERS - 1:
                    update_lo(p, q, 0)
                if ahead:
                    ln_mean_var(m)
                if q < ITEMS - 1 or not last:
                    copy_turned_lo(p, q + 1)
                if ahead:
                    dve.wait_ge(ln_aggr, SC * graphs(p + 1, m))
                    ln_eps(m)
                    dve.wait_ge(adj_loaded[m], loads(p + 1))
                    make_mask(m)
                    dve.wait_ge(ln_rstd_ready, graphs(p + 1, m))
                    ln_scale(m)
                pre_n(p, q, 1)
                if ahead:
                    dve.wait_ge(ln_rs_ready, graphs(p + 1, m))
                    ln_center(m)
                update(p, q, 1)
                if l < LAYERS - 1:
                    update_lo(p, q, 1)
                if ahead:
                    dve.wait_ge(ln_hi_ready, graphs(p + 1, m))
                    ln_lo(m)

            def pair(p, first=False, last=False):
                for q in range(ITEMS):
                    item(p, q, first, last)

            def first_ln(m):
                dve.wait_ge(x_loaded[m], 16)
                ln_statistics(m)
                dve.wait_ge(ln_stats, SC * (m + 1))
                ln_mean_var(m)
                dve.wait_ge(ln_aggr, SC * (m + 1))
                ln_eps(m)

            dve.wait_ge(w_loaded, 32)
            dve.tensor_reduce(wmax[:, 0:1], w_sb[:, :, :, :].rearrange("p a b c -> p (a b c)"), AX.X, ALU.max,
                              apply_absolute_value=True).then_inc(wmax_ready, 1)
            dve.tensor_reduce(wmax[:, 1:2], wih_sb[:, :, :].rearrange("p a b -> p (a b)"), AX.X, ALU.max,
                              apply_absolute_value=True).then_inc(wmax_ready, 1)
            first_ln(0)
            dve.wait_ge(whh_loaded, 16)
            dve.tensor_reduce(wmax[:, 2:3], whh_sb[:, :, :].rearrange("p a b -> p (a b)"), AX.X, ALU.max,
                              apply_absolute_value=True).then_inc(wmax_ready, 1)
            dve.wait_ge(ln_rstd_ready, 1)
            ln_scale(0)
            dve.wait_ge(ln_rs_ready, 1)
            ln_center(0)
            dve.wait_ge(wmax_all_ready, 1)
            dve.scalar_tensor_tensor(out=bound[:, 0:1], in0=wmax_all[:, 0:1], scalar=D / AGG_SCALE,
                                     in1=wmax_all[:, 1:2], op0=ALU.mult, op1=ALU.mult).then_inc(scale_step, 1)
            dve.wait_ge(scale_step, 1)
            dve.scalar_tensor_tensor(out=bound[:, 1:2], in0=wmax_all[:, 2:3], scalar=1.0 / H_SCALE,
                                     in1=bound[:, 0:1], op0=ALU.mult, op1=ALU.max).then_inc(scale_step, 1)
            dve.wait_ge(scale_step, 2)
            dve.tensor_scalar(bound[:, 0:1], bound[:, 1:2], 1e-30, None, ALU.max).then_inc(scale_step, 1)
            dve.wait_ge(scale_step, 3)
            dve.tensor_scalar(pow2[:, :].bitcast(I32), bound[:, 0:1].bitcast(I32), POW2_BITS, None,
                              ALU.bitwise_and).then_inc(scale_step, 1)
            dve.wait_ge(scale_step, 4)
            dve.reciprocal(rpow2[:, :], pow2[:, :]).then_inc(scale_step, 1)
            dve.wait_ge(scale_step, 5)
            dve.tensor_scalar(wx_scale[:, :], rpow2[:, :], 2.0 ** 14 / AGG_SCALE, None,
                              ALU.mult).then_inc(scales_ready, 1)
            dve.tensor_scalar(wh_scale[:, :], rpow2[:, :], 2.0 ** 14 / H_SCALE, None,
                              ALU.mult).then_inc(scales_ready, 1)
            dve.tensor_scalar(gate_scale[:, :], rpow2[:, :], 2.0 ** 14, None, ALU.mult).then_inc(scales_ready, 1)
            dve.tensor_scalar(gate_unscale[:, :], pow2[:, :], 2.0 ** -14, None, ALU.mult).then_inc(scales_ready, 1)
            dve.wait_ge(b_loaded, 32)
            dve.tensor_tensor(bsum[:, :], bih_sb[:, :], bhh_sb[:, :], ALU.add).then_inc(biases_ready, 1)
            dve.wait_ge(scales_ready, 4)
            dve.tensor_scalar(bhn[:, :], bhh_sb[:, 2 * DC:3 * DC], gate_scale[:, 0:1], None,
                              ALU.mult).then_inc(biases_ready, 1)
            dve.wait_ge(ln_hi_ready, 1)
            ln_lo(0)
            dve.wait_ge(adj_loaded[0], 16)
            make_mask(0)
            dve.wait_ge(wh_hi_ready, 1)
            dve.scalar_tensor_tensor(out=wh_lo[:, :, :], in0=whh_sb[:, :, :], scalar=wh_scale[:, 0:1],
                                     in1=wh_hi[:, :, :], op0=ALU.mult, op1=ALU.subtract).then_inc(wh_lo_ready, 1)
            for n in range(WPRODS):
                l, c, g = n // (2 * DC), n // 2 % DC, n % 2
                dve.wait_ge(prod_hi_ready, n + 1)
                dve.scalar_tensor_tensor(out=wx_lo[:, l, c, g * WCOLS:(g + 1) * WCOLS],
                                         in0=prod_ps[n % 4][:, 0:WCOLS], scalar=wx_scale[:, 0:1],
                                         in1=wx_hi[:, l, c, g * WCOLS:(g + 1) * WCOLS], op0=ALU.mult,
                                         op1=ALU.subtract).then_inc(prod_lo_ready, 1)
            copy_turned_lo(0, 0)
            first_ln(1)
            dve.wait_ge(adj_loaded[1], 16)
            make_mask(1)
            dve.wait_ge(ln_rstd_ready, 2)
            ln_scale(1)
            dve.wait_ge(ln_rs_ready, 2)
            ln_center(1)
            dve.wait_ge(ln_hi_ready, 2)
            ln_lo(1)
            dve.wait_ge(biases_ready, 2)
            pair(0, first=True)
            with dve.Fori(1, PAIRS - 1) as p:
                pair(p)
            pair(PAIRS - 1, last=True)
            for m in range(2):
                add_out(PAIRS - 1, m)

        @block.tensor
        def _(pe):
            def turn(p, q):
                l, m = q % ITEMS // 2, q % 2
                for i, (nat, tr, done) in enumerate(((nat_hi[m], hT_hi[m][l % 2], turned_hi),
                                                     (nat_lo[m], hT_lo[m][l % 2], turned_lo))):
                    for c in range(SC):
                        for d in range(DC):
                            if l == 0:
                                at, src = d * N + c * P, nat[:, c, d * P:(d + 1) * P]
                            else:
                                at, src = c * D + d * P, tr[:, d, c * P:(c + 1) * P]
                            last = pe.transpose(turn_h[i][:, at:at + P], src, ident_h[:, :])
                    last.then_inc(done, 1)

            def turn_out(m):
                for i in range(2):
                    for c in range(SC // 2):
                        for d in range(DC):
                            at = c * D + d * P
                            t0 = (i * SC // 2 + c) * P
                            last = pe.transpose(turn_ps[i][:, at:at + P], hT[m][:, d, t0:t0 + P], ident_f[:, :])
                    last.then_inc(out_turned, 1)

            def hidden(dst, l, m, g, stop):
                hi, lo = hT_hi[m][l % 2], hT_lo[m][l % 2]
                cols = slice(g * P, (g + 1) * P)
                for d in range(DC):
                    pe.matmul(dst[:, :], wh_hi[:, d, cols], hi[:, d, :], start=d == 0, stop=False)
                    pe.matmul(dst[:, :], wh_hi[:, d, cols], lo[:, d, :], start=False, stop=False)
                    last = pe.matmul(dst[:, :], wh_lo[:, d, cols], hi[:, d, :], start=False,
                                     stop=stop and d == DC - 1)
                return last

            def incoming(dst, l, g, start):
                cols = slice(g * P, (g + 1) * P)
                for d in range(DC):
                    pe.matmul(dst[:, :], wx_hi[:, l, d, cols], agg_hi[:, d, :], start=start and d == 0, stop=False)
                    pe.matmul(dst[:, :], wx_lo[:, l, d, cols], agg_hi[:, d, :], start=False, stop=False)
                    last = pe.matmul(dst[:, :], wx_hi[:, l, d, cols], agg_lo[:, d, :], start=False,
                                     stop=d == DC - 1)
                return last

            def item(p, q, first, last):
                l, m = q // 2, q % 2
                before = not (first and q == 0)
                if q < 2 and not first:
                    pe.wait_ge(turned_hi_copied, items(p, q))
                    pe.wait_ge(turned_lo_copied, items(p, q))
                    pe.wait_ge(h_new, halves(p - 1, ITEMS - 2 + m, DC - 1))
                    turn_out(m)
                if l == 0:
                    pe.wait_ge(mask_ready, graphs(p, m))
                else:
                    pe.wait_ge(turned_hi_copied, items(p, q))
                    pe.wait_ge(turned_lo_copied, items(p, q))
                for j in range(DC):
                    cols = slice(j * P, (j + 1) * P)
                    for c in range(SC):
                        pe.matmul(agg_ps[j][:, :], nat_hi[m][:, c, cols], mask[m][:, c, :],
                                  start=c == 0, stop=False)
                        mm = pe.matmul(agg_ps[j][:, :], nat_lo[m][:, c, cols], mask[m][:, c, :],
                                       start=False, stop=c == SC - 1)
                    mm.then_inc(agg_ready, 1)
                if l == 0:
                    pe.wait_ge(turned_hi_copied, items(p, q))
                    pe.wait_ge(turned_lo_copied, items(p, q))
                if before:
                    pe.wait_ge(pre_ready, halves(p, q - 1, DC - 1))
                hidden(hn_ps, l, m, 2 * DC, True).then_inc(hn_ready, 1)
                hidden(r_ps, l, m, 0, False)
                if before:
                    pe.wait_ge(z_sig, halves(p, q - 1, DC - 1))
                hidden(z_ps, l, m, DC, False)
                pe.wait_ge(agg_hi_ready, halves(p, q, DC - 1))
                pe.wait_ge(agg_lo_ready, halves(p, q, DC - 1))
                incoming(r_ps, l, 0, False).then_inc(r_ready, 1)
                incoming(in_ps, l, 2 * DC, True).then_inc(in_ready, 1)
                incoming(z_ps, l, DC, False).then_inc(z_ready, 1)
                if q < ITEMS - 1 or not last:
                    nl = (q + 1) % ITEMS // 2
                    nm = (q + 1) % 2
                    if nl == 0:
                        pe.wait_ge(ln_hi_ready, graphs(p + (q + 1) // ITEMS, nm))
                        pe.wait_ge(ln_lo_ready, graphs(p + (q + 1) // ITEMS, nm))
                    else:
                        pe.wait_ge(h_hi_ready, splits(p, q - 1, DC - 1))
                        pe.wait_ge(h_lo_ready, splits(p, q - 1, DC - 1))
                    if q < 2 and not first:
                        pe.wait_ge(out_added, 2 * graphs(p - 1, m))
                    turn(p, q + 1)
                pe.wait_ge(r_sig, halves(p, q, 0))
                hidden(r_ps, l, m, 1, False)
                incoming(r_ps, l, 1, False).then_inc(r_ready, 1)
                pe.wait_ge(gated, halves(p, q, 0))
                hidden(hn_ps, l, m, 2 * DC + 1, True).then_inc(hn_ready, 1)
                pe.wait_ge(pre_ready, halves(p, q, 0))
                incoming(in_ps, l, 2 * DC + 1, True).then_inc(in_ready, 1)
                pe.wait_ge(z_sig, halves(p, q, 0))
                hidden(z_ps, l, m, DC + 1, False)
                incoming(z_ps, l, DC + 1, False).then_inc(z_ready, 1)

            def pair(p, first=False, last=False):
                for q in range(ITEMS):
                    item(p, q, first, last)

            pe.wait_ge(w_loaded, 32)
            for n in range(WPRODS):
                l, c, g = n // (2 * DC), n // 2 % DC, n % 2
                if n >= 4:
                    pe.wait_ge(prod_lo_ready, n - 3)
                for e in range(DC):
                    mm = pe.matmul(prod_ps[n % 4][:, 0:WCOLS], w_sb[:, l, e, c * P:(c + 1) * P],
                                   wih_sb[:, e, g * WCOLS:(g + 1) * WCOLS], start=e == 0, stop=e == DC - 1)
                mm.then_inc(prod_ready, 1)
            pe.wait_ge(consts_ready, 2)
            pe.wait_ge(ln_hi_ready, 1)
            pe.wait_ge(ln_lo_ready, 1)
            turn(0, 0)
            pe.wait_ge(wh_lo_ready, 1)
            pe.wait_ge(prod_lo_ready, WPRODS)
            pair(0, first=True)
            with pe.Fori(1, PAIRS - 1) as p:
                pair(p)
            pair(PAIRS - 1, last=True)
            pe.wait_ge(h_new, halves(PAIRS - 1, ITEMS - 2, DC - 1))
            turn_out(0)
            pe.wait_ge(h_new, halves(PAIRS - 1, ITEMS - 1, DC - 1))
            pe.wait_ge(out_added, 2 * graphs(PAIRS - 1, 0))
            turn_out(1)


def kernel(x, adj, L0_gnn_weight, L0_gnn_w_ih, L0_gnn_w_hh, L0_gnn_b_ih, L0_gnn_b_hh):
    import numpy as np
    import concourse.bacc as bacc
    from concourse.bass_utils import run_bass_kernel_spmd

    arrays = {
        "x": np.ascontiguousarray(x),
        "adj": np.ascontiguousarray(adj),
        "w_t": np.ascontiguousarray(np.transpose(L0_gnn_weight, (0, 2, 1))),
        "wih_t": np.ascontiguousarray(np.transpose(L0_gnn_w_ih)),
        "whh_t": np.ascontiguousarray(np.transpose(L0_gnn_w_hh)),
        "bih": np.ascontiguousarray(np.transpose(np.reshape(L0_gnn_b_ih, (-1, P)))),
        "bhh": np.ascontiguousarray(np.transpose(np.reshape(L0_gnn_b_hh, (-1, P)))),
    }
    nc = bacc.Bacc("TRN2", target_bir_lowering=False, num_devices=1)
    args = [nc.dram_tensor(k, a.shape, mybir.dt.from_np(a.dtype), kind="ExternalInput").ap()
            for k, a in arrays.items()]
    args.append(nc.dram_tensor("out", x.shape, F32, kind="ExternalOutput").ap())
    gnn_kernel(nc, *args)
    r = run_bass_kernel_spmd(nc, [arrays], core_ids=[0])
    return r.results[0]["out"]
```

```python
from contextlib import ExitStack

import concourse.bass as bass
from concourse import mybir

F32 = mybir.dt.float32
F16 = mybir.dt.float16
I32 = mybir.dt.int32
ALU = mybir.AluOpType
ACT = mybir.ActivationFunctionType
AX = mybir.AxisListType

P = 128
H_SCALE = 2.0 ** 11
AGG_SCALE = 2.0 ** 2
LN_EPS = 1e-5
WARM_UP = 40
POW2_BITS = 0x7F800000


def gnn_kernel(nc, x, adj, w_t, wih_t, whh_t, bih, bhh, out):
    B, N, D = x.shape
    LAYERS = w_t.shape[0]
    GATES = wih_t.shape[1]
    SC = N // P
    DC = D // P
    GC = GATES // P
    PAIRS = B // 2
    ITEMS = 2 * LAYERS
    SPLITS = ITEMS - 2
    WCOLS = GATES // 2
    WPRODS = LAYERS * DC * 2
    PER_LAYER = DC * 2
    assert LAYERS == 3 and DC == 2 and SC == 4 and GATES == 3 * D and B % 2 == 0 and PAIRS > 2

    ctx = ExitStack()
    with ctx:
        def sb(name, shape, dt):
            return ctx.enter_context(nc.sbuf_tensor(name, shape, dt))

        def bank(name, shape, dt):
            return ctx.enter_context(nc.psum_tensor(name, shape, dt))

        def sem(name):
            return ctx.enter_context(nc.semaphore(name))

        w_sb = sb("w_sb", [P, LAYERS, DC, D], F32)
        wih_sb = sb("wih_sb", [P, DC, GATES], F32)
        whh_sb = sb("whh_sb", [P, DC, GATES], F32)
        wx_hi = sb("wx_hi", [P, LAYERS, DC, GATES], F16)
        wx_lo = sb("wx_lo", [P, LAYERS, DC, GATES], F16)
        wh_hi = sb("wh_hi", [P, DC, GATES], F16)
        wh_lo = sb("wh_lo", [P, DC, GATES], F16)
        prod_sb = sb("prod_sb", [P, LAYERS - 1, DC, GATES], F32)
        whs_sb = sb("whs_sb", [P, DC, GATES], F32)
        bih_sb = sb("bih_sb", [P, GC], F32)
        bhh_sb = sb("bhh_sb", [P, GC], F32)
        bsum = sb("bsum", [P, GC], F32)
        bhn = sb("bhn", [P, DC], F32)
        ident_h = sb("ident_h", [P, P], F16)
        ident_f = sb("ident_f", [P, P], F32)
        minus_half = sb("minus_half", [P, SC], F32)
        wmax = sb("wmax", [P, 3], F32)
        wmax_all = sb("wmax_all", [P, 3], F32)
        bound = sb("bound", [P, 2], F32)
        pow2 = sb("pow2", [P, 1], F32)
        rpow2 = sb("rpow2", [P, 1], F32)
        gate_unscale = sb("gate_unscale", [P, 1], F32)
        gate_scale = sb("gate_scale", [P, 1], F32)
        wx_scale = sb("wx_scale", [P, 1], F32)
        wh_scale = sb("wh_scale", [P, 1], F32)

        adj_in = [sb(f"adj_in{m}", [P, SC, N], I32) for m in range(2)]
        mask = [sb(f"mask{m}", [P, SC, N], F16) for m in range(2)]
        x_in = [sb(f"x_in{m}", [P, SC, D], F32) for m in range(2)]
        x_out = [sb(f"x_out{m}", [P, SC, D], F32) for m in range(2)]
        nat_hi = [sb(f"nat_hi{m}", [P, SC, D], F16) for m in range(2)]
        nat_lo = [sb(f"nat_lo{m}", [P, SC, D], F16) for m in range(2)]
        hT_hi = [[sb(f"hT_hi{m}_{s}", [P, DC, N], F16) for s in range(2)] for m in range(2)]
        hT_lo = [[sb(f"hT_lo{m}_{s}", [P, DC, N], F16) for s in range(2)] for m in range(2)]
        hT = [sb(f"hT{m}", [P, DC, N], F32) for m in range(2)]
        ln_st = [sb(f"ln_st{m}", [P, SC, 6], F32) for m in range(2)]
        ln_mv = [sb(f"ln_mv{m}", [P, SC, 2], F32) for m in range(2)]
        ln_ve = [sb(f"ln_ve{m}", [P, SC], F32) for m in range(2)]
        ln_rstd = [sb(f"ln_rstd{m}", [P, SC], F32) for m in range(2)]
        ln_rs = [sb(f"ln_rs{m}", [P, SC], F32) for m in range(2)]
        ln_y = [sb(f"ln_y{m}", [P, SC, D], F32) for m in range(2)]

        agg_hi = sb("agg_hi", [P, DC, N], F16)
        agg_lo = sb("agg_lo", [P, DC, N], F16)
        r_sb = sb("r_sb", [P, DC, N], F32)
        z_sb = sb("z_sb", [P, DC, N], F32)
        n_sb = sb("n_sb", [P, DC, N], F32)
        pre_sb = sb("pre_sb", [P, DC, N], F32)
        dif_sb = sb("dif_sb", [P, DC, N], F32)

        agg_ps = [bank(f"agg_ps{j}", [P, N], F32) for j in range(DC)]
        r_ps = bank("r_ps", [P, N], F32)
        z_ps = bank("z_ps", [P, N], F32)
        in_ps = bank("in_ps", [P, N], F32)
        hn_ps = bank("hn_ps", [P, N], F32)
        turn_ps = [bank(f"turn_ps{i}", [P, 512], F32) for i in range(2)]
        turn_h = [t[:, :].bitcast(F16) for t in turn_ps]
        prod_ps = [r_ps, z_ps, in_ps, hn_ps, turn_ps[0], turn_ps[1], agg_ps[0], agg_ps[1]]

        w0_loaded = sem("w0_loaded")
        w_loaded = sem("w_loaded")
        wih_loaded = [sem(f"wih_loaded{g}") for g in range(2)]
        whh_loaded = sem("whh_loaded")
        b_loaded = sem("b_loaded")
        consts_cleared = sem("consts_cleared")
        consts_ready = sem("consts_ready")
        wmax_ready = sem("wmax_ready")
        wmax_all_ready = sem("wmax_all_ready")
        scale_step = sem("scale_step")
        scales_ready = sem("scales_ready")
        biases_ready = sem("biases_ready")
        prod_ready = sem("prod_ready")
        prod_copied = sem("prod_copied")
        wx_hi_ready = sem("wx_hi_ready")
        wx_lo_ready = sem("wx_lo_ready")
        whs_ready = sem("whs_ready")
        wh_hi_ready = sem("wh_hi_ready")
        wh_lo_ready = sem("wh_lo_ready")
        x_loaded = [sem(f"x_loaded{m}") for m in range(2)]
        adj_loaded = [sem(f"adj_loaded{m}") for m in range(2)]
        stored = [sem(f"stored{m}") for m in range(2)]
        x_copied = sem("x_copied")
        mask_ready = sem("mask_ready")
        ln_stats = sem("ln_stats")
        ln_aggr = sem("ln_aggr")
        ln_eps_added = sem("ln_eps_added")
        ln_rstd_ready = sem("ln_rstd_ready")
        ln_rs_ready = sem("ln_rs_ready")
        ln_centered = sem("ln_centered")
        ln_hi_ready = sem("ln_hi_ready")
        ln_lo_ready = sem("ln_lo_ready")
        h0_summed = sem("h0_summed")
        out_turned = sem("out_turned")
        out_added = sem("out_added")
        turned_hi = sem("turned_hi")
        turned_lo = sem("turned_lo")
        turned_hi_copied = sem("turned_hi_copied")
        turned_lo_copied = sem("turned_lo_copied")
        agg_ready = sem("agg_ready")
        r_ready = sem("r_ready")
        z_ready = sem("z_ready")
        in_ready = sem("in_ready")
        hn_ready = sem("hn_ready")
        agg_hi_ready = sem("agg_hi_ready")
        agg_lo_ready = sem("agg_lo_ready")
        r_sig = sem("r_sig")
        z_sig = sem("z_sig")
        n_tanh = sem("n_tanh")
        gated = sem("gated")
        pre_ready = sem("pre_ready")
        dif_ready = sem("dif_ready")
        zdif_ready = sem("zdif_ready")
        h_new = sem("h_new")
        h_hi_ready = sem("h_hi_ready")
        h_lo_ready = sem("h_lo_ready")

        def graphs(p, m):
            return 2 * p + (m + 1)

        def loads(p):
            return 16 * p + 16

        def items(p, q):
            return ITEMS * p + (q + 1)

        def halves(p, q, j):
            return DC * ITEMS * p + (DC * q + j + 1)

        def splits(p, q, j):
            return DC * SPLITS * p + (DC * q + j + 1)

        def product(n):
            l, c, g = n // PER_LAYER, n // 2 % DC, n % 2
            return l, c, slice(g * WCOLS, (g + 1) * WCOLS)

        def product_bank(n):
            return prod_ps[n if n < PER_LAYER else PER_LAYER + n % PER_LAYER][:, 0:WCOLS]

        def pairs_between(engine):
            return nc.Fori(1, PAIRS - 1, engines=(engine,), hint_back_edge=True)

        block = ctx.enter_context(nc.Block())

        @block.sync
        def _(sp):
            def graph(t, p, m):
                return t[bass.ds(2 * p + m, 1)].rearrange("b (c p) f -> (b p) c f", p=P)

            def load_adj(p, m):
                sp.dma_start(adj_in[m][:, :, :], graph(adj, p, m)).then_inc(adj_loaded[m], 16)

            def load_x(p, m):
                sp.dma_start(x_in[m][:, :, :], graph(x, p, m)).then_inc(x_loaded[m], 16)

            def store(p, m):
                sp.wait_ge(out_added, 2 * graphs(p, m))
                sp.dma_start(graph(out, p, m), x_out[m][:, :, :]).then_inc(stored[m], 16)

            def pair(p, first=False, last=False):
                if not last:
                    for m in range(2):
                        sp.wait_ge(mask_ready, graphs(p, m))
                        load_adj(p + 1, m)
                if not first:
                    for m in range(2):
                        store(p - 1, m)
                if not last:
                    for m in range(2):
                        sp.wait_ge(x_copied, graphs(p, m))
                        load_x(p + 1, m)

            w_v = w_t.rearrange("l (c p) d -> p l c d", p=P)
            sp.dma_start(w_sb[:, 0, :, :], w_v[:, 0, :, :]).then_inc(w0_loaded, 16)
            wih_v = wih_t.rearrange("(c p) g -> p c g", p=P)
            for g in range(2):
                cols = slice(g * WCOLS, (g + 1) * WCOLS)
                sp.dma_start(wih_sb[:, :, cols], wih_v[:, :, cols]).then_inc(wih_loaded[g], 16)
            for l in range(1, LAYERS):
                sp.dma_start(w_sb[:, l, :, :], w_v[:, l, :, :]).then_inc(w_loaded, 16)
            sp.dma_start(whh_sb[:, :, :], whh_t.rearrange("(c p) g -> p c g", p=P)).then_inc(whh_loaded, 16)
            load_x(0, 0)
            sp.dma_start(bih_sb[:, :], bih).then_inc(b_loaded, 16)
            sp.dma_start(bhh_sb[:, :], bhh).then_inc(b_loaded, 16)
            load_adj(0, 0)
            load_x(0, 1)
            load_adj(0, 1)
            pair(0, first=True)
            with sp.Fori(1, PAIRS - 1) as p:
                pair(p)
            pair(PAIRS - 1, last=True)
            for m in range(2):
                store(PAIRS - 1, m)
            for m in range(2):
                sp.wait_ge(stored[m], loads(PAIRS - 1))

        @block.gpsimd
        def _(pool):
            pool.memset(ident_h[:, :], 0.0).then_inc(consts_cleared, 1)
            pool.memset(ident_f[:, :], 0.0).then_inc(consts_cleared, 1)
            pool.memset(minus_half[:, :], -0.5).then_inc(consts_cleared, 1)
            pool.wait_ge(consts_cleared, 3)
            for t in (ident_h, ident_f):
                pool.affine_select(out=t[:, :], in_=t[:, :], compare_op=ALU.not_equal, fill=1.0, base=0,
                                   pattern=[[-1, P]], channel_multiplier=1).then_inc(consts_ready, 1)

            def rstd(p, m):
                pool.wait_ge(ln_eps_added, graphs(p, m))
                pool.tensor_tensor(ln_rstd[m][:, :], ln_ve[m][:, :], minus_half[:, :],
                                   ALU.pow).then_inc(ln_rstd_ready, 1)

            rstd(0, 0)
            pool.wait_ge(wmax_ready, 3)
            pool.partition_all_reduce(wmax_all[:, :], wmax[:, :], P,
                                      bass.bass_isa.ReduceOp.max).then_inc(wmax_all_ready, 1)
            rstd(0, 1)
            pool.wait_ge(whs_ready, 1)
            pool.wait_ge(wh_hi_ready, 1)
            pool.tensor_tensor(wh_lo[:, :, :], whs_sb[:, :, :], wh_hi[:, :, :],
                               ALU.subtract).then_inc(wh_lo_ready, 1)
            rstd(1, 0)
            rstd(1, 1)
            with pool.Fori(1, PAIRS - 1) as p:
                for m in range(2):
                    rstd(p + 1, m)

        @block.scalar
        def _(act):
            def ln_hi(m):
                act.activation(nat_hi[m][:, :, :], ln_y[m][:, :, :], ACT.Relu).then_inc(ln_hi_ready, 1)

            def copy_turned_hi(l, m):
                dst = hT_hi[m][0] if l == 0 else nat_hi[m]
                act.activation(dst[:, :, :].rearrange("p a b -> p (a b)"), turn_h[0],
                               ACT.Copy).then_inc(turned_hi_copied, 1)

            def copy_x(p, m, first):
                act.wait_ge(x_loaded[m], loads(p))
                if not first:
                    act.wait_ge(stored[m], loads(p - 1))
                act.activation(x_out[m][:, :, :], x_in[m][:, :, :], ACT.Copy).then_inc(x_copied, 1)

            def gates(p, q, j):
                l, m = q // 2, q % 2
                act.wait_ge(r_ready, halves(p, q, j))
                act.activation(r_sb[:, j, :], r_ps[:, :], ACT.Sigmoid, bias=bsum[:, j:j + 1],
                               scale=gate_unscale[:, 0:1]).then_inc(r_sig, 1)
                act.wait_ge(pre_ready, halves(p, q, j))
                act.activation(n_sb[:, j, :], pre_sb[:, j, :], ACT.Tanh, bias=bih_sb[:, 2 * DC + j:2 * DC + j + 1],
                               scale=gate_unscale[:, 0:1]).then_inc(n_tanh, 1)
                act.wait_ge(z_ready, halves(p, q, j))
                act.activation(z_sb[:, j, :], z_ps[:, :], ACT.Sigmoid, bias=bsum[:, DC + j:DC + j + 1],
                               scale=gate_unscale[:, 0:1]).then_inc(z_sig, 1)
                if l < LAYERS - 1:
                    act.wait_ge(h_new, halves(p, q, j))
                    act.activation(hT_hi[m][(l + 1) % 2][:, j, :], hT[m][:, j, :], ACT.Copy,
                                   scale=H_SCALE).then_inc(h_hi_ready, 1)

            def item(p, q, first, last):
                m = q % 2
                for j in range(DC):
                    act.wait_ge(agg_ready, halves(p, q, j))
                    act.activation(agg_hi[:, j, :], agg_ps[j][:, :], ACT.Copy,
                                   scale=AGG_SCALE / H_SCALE).then_inc(agg_hi_ready, 1)
                if 2 <= q < 4:
                    copy_x(p, m, first)
                gates(p, q, 0)
                if first and q + 1 < LAYERS:
                    act.activation(wx_hi[:, q + 1, :, :], prod_sb[:, q, :, :], ACT.Copy,
                                   scale=wx_scale[:, 0:1]).then_inc(wx_hi_ready, 1)
                if q < ITEMS - 1 or not last:
                    act.wait_ge(turned_hi, items(p, q + 1))
                    copy_turned_hi((q + 1) % ITEMS // 2, (q + 1) % 2)
                gates(p, q, 1)
                if q >= ITEMS - 2 and not last:
                    act.wait_ge(ln_centered, graphs(p + 1, m))
                    ln_hi(m)

            def pair(p, first=False, last=False):
                for q in range(ITEMS):
                    item(p, q, first, last)

            def copy_product(n):
                l, c, cols = product(n)
                act.wait_ge(prod_ready, n + 1)
                act.activation(prod_sb[:, l - 1, c, cols], product_bank(n), ACT.Copy).then_inc(prod_copied, 1)

            def split_product(n):
                l, c, cols = product(n)
                act.activation(wx_hi[:, l, c, cols], product_bank(n), ACT.Copy,
                               scale=wx_scale[:, 0:1]).then_inc(wx_hi_ready, 1)

            copy_product(4)
            copy_product(5)
            act.wait_ge(scales_ready, 4)
            split_product(0)
            copy_product(6)
            split_product(1)
            split_product(2)
            copy_product(7)
            split_product(3)
            act.wait_ge(ln_centered, 1)
            ln_hi(0)
            copy_product(8)
            copy_product(9)
            act.activation(wh_hi[:, :, :], whh_sb[:, :, :], ACT.Copy,
                           scale=wh_scale[:, 0:1]).then_inc(wh_hi_ready, 1)
            copy_product(10)
            copy_product(11)
            act.activation(whs_sb[:, :, :], whh_sb[:, :, :], ACT.Copy,
                           scale=wh_scale[:, 0:1]).then_inc(whs_ready, 1)
            act.wait_ge(turned_hi, 1)
            copy_turned_hi(0, 0)
            act.wait_ge(ln_centered, 2)
            ln_hi(1)
            act.wait_ge(biases_ready, 2)
            pair(0, first=True)
            with pairs_between(mybir.EngineType.Activation) as p:
                pair(p)
            pair(PAIRS - 1, last=True)

        @block.vector
        def _(dve):
            def ln_statistics(m):
                for c in range(SC):
                    dve.bn_stats(ln_st[m][:, c, :], x_in[m][:, c, :]).then_inc(ln_stats, 1)

            def ln_mean_var(m):
                for c in range(SC):
                    dve.bn_aggr(ln_mv[m][:, c, :], ln_st[m][:, c, :]).then_inc(ln_aggr, 1)

            def ln_eps(m):
                dve.tensor_scalar(ln_ve[m][:, :], ln_mv[m][:, :, 1], LN_EPS, None, ALU.add).then_inc(ln_eps_added, 1)

            def ln_scale(m):
                dve.tensor_scalar(ln_rs[m][:, :], ln_rstd[m][:, :], H_SCALE, None, ALU.mult).then_inc(ln_rs_ready, 1)

            def ln_center(m):
                for c in range(SC):
                    last = dve.tensor_scalar(ln_y[m][:, c, :], x_in[m][:, c, :], ln_mv[m][:, c, 0:1],
                                             ln_rs[m][:, c:c + 1], ALU.subtract, ALU.mult)
                last.then_inc(ln_centered, 1)

            def ln_lo(m):
                dve.scalar_tensor_tensor(out=nat_lo[m][:, :, :], in0=ln_y[m][:, :, :], scalar=0.0,
                                         in1=nat_hi[m][:, :, :], op0=ALU.max, op1=ALU.subtract).then_inc(ln_lo_ready, 1)

            def make_mask(m):
                dve.tensor_scalar(mask[m][:, :, :], adj_in[m][:, :, :], 0.0, None,
                                  ALU.not_equal).then_inc(mask_ready, 1)

            def copy_turned_lo(p, q):
                l, m = q % ITEMS // 2, q % 2
                dst = hT_lo[m][0] if l == 0 else nat_lo[m]
                dve.wait_ge(turned_lo, items(p, q))
                dve.tensor_copy(dst[:, :, :].rearrange("p a b -> p (a b)"), turn_h[1]).then_inc(turned_lo_copied, 1)

            def sum_h0(p, m):
                dve.wait_ge(turned_hi_copied, items(p, m))
                dve.wait_ge(turned_lo_copied, items(p, m))
                dve.tensor_tensor(hT[m][:, :, :], hT_hi[m][0][:, :, :], hT_lo[m][0][:, :, :],
                                  ALU.add).then_inc(h0_summed, 1)

            def add_out(p, m):
                for i in range(2):
                    dve.wait_ge(out_turned, 2 * graphs(p, m) + (i - 1))
                    part = x_out[m][:, i * SC // 2:(i + 1) * SC // 2, :].rearrange("p c f -> p (c f)")
                    dve.tensor_tensor(part, turn_ps[i][:, :], part, ALU.add).then_inc(out_added, 1)

            def pre_n(p, q, j):
                dve.wait_ge(r_sig, halves(p, q, j))
                dve.wait_ge(hn_ready, halves(p, q, j))
                dve.scalar_tensor_tensor(out=pre_sb[:, j, :], in0=hn_ps[:, :], scalar=bhn[:, j:j + 1],
                                         in1=r_sb[:, j, :], op0=ALU.add, op1=ALU.mult).then_inc(gated, 1)
                dve.wait_ge(in_ready, halves(p, q, j))
                dve.wait_ge(gated, halves(p, q, j))
                dve.tensor_tensor(pre_sb[:, j, :], in_ps[:, :], pre_sb[:, j, :], ALU.add).then_inc(pre_ready, 1)

            def update(p, q, j):
                l, m = q // 2, q % 2
                dve.wait_ge(n_tanh, halves(p, q, j))
                if l == 0:
                    dve.wait_ge(h0_summed, graphs(p, m))
                    dve.scalar_tensor_tensor(out=dif_sb[:, j, :], in0=hT[m][:, j, :], scalar=1.0 / H_SCALE,
                                             in1=n_sb[:, j, :], op0=ALU.mult, op1=ALU.subtract).then_inc(dif_ready, 1)
                else:
                    dve.tensor_tensor(dif_sb[:, j, :], hT[m][:, j, :], n_sb[:, j, :],
                                      ALU.subtract).then_inc(dif_ready, 1)
                dve.wait_ge(z_sig, halves(p, q, j))
                dve.wait_ge(dif_ready, halves(p, q, j))
                dve.tensor_tensor(dif_sb[:, j, :], z_sb[:, j, :], dif_sb[:, j, :], ALU.mult).then_inc(zdif_ready, 1)
                dve.wait_ge(zdif_ready, halves(p, q, j))
                dve.tensor_tensor(hT[m][:, j, :], n_sb[:, j, :], dif_sb[:, j, :], ALU.add).then_inc(h_new, 1)

            def update_lo(p, q, j):
                l, m = q // 2, q % 2
                dve.wait_ge(h_hi_ready, splits(p, q, j))
                dve.scalar_tensor_tensor(out=hT_lo[m][(l + 1) % 2][:, j, :], in0=hT[m][:, j, :], scalar=H_SCALE,
                                         in1=hT_hi[m][(l + 1) % 2][:, j, :], op0=ALU.mult,
                                         op1=ALU.subtract).then_inc(h_lo_ready, 1)

            def item(p, q, first, last):
                l, m = q // 2, q % 2
                ahead = q >= ITEMS - 2 and not last
                for j in range(DC):
                    dve.wait_ge(agg_hi_ready, halves(p, q, j))
                    dve.scalar_tensor_tensor(out=agg_lo[:, j, :], in0=agg_ps[j][:, :], scalar=AGG_SCALE / H_SCALE,
                                             in1=agg_hi[:, j, :], op0=ALU.mult,
                                             op1=ALU.subtract).then_inc(agg_lo_ready, 1)
                if q < 2 and not first:
                    add_out(p - 1, m)
                if l == 0:
                    sum_h0(p, m)
                if first and q == 0:
                    dve.wait_ge(ln_hi_ready, 2)
                    ln_lo(1)
                if ahead:
                    dve.wait_ge(x_loaded[m], loads(p + 1))
                    ln_statistics(m)
                pre_n(p, q, 0)
                if ahead:
                    dve.wait_ge(ln_stats, SC * graphs(p + 1, m))
                update(p, q, 0)
                if l < LAYERS - 1:
                    update_lo(p, q, 0)
                if ahead:
                    ln_mean_var(m)
                if q < ITEMS - 1 or not last:
                    copy_turned_lo(p, q + 1)
                if first and q == 0:
                    dve.wait_ge(adj_loaded[1], 16)
                    make_mask(1)
                if first and q + 1 < LAYERS:
                    dve.wait_ge(wx_hi_ready, PER_LAYER + q + 1)
                    dve.scalar_tensor_tensor(out=wx_lo[:, q + 1, :, :], in0=prod_sb[:, q, :, :],
                                             scalar=wx_scale[:, 0:1], in1=wx_hi[:, q + 1, :, :], op0=ALU.mult,
                                             op1=ALU.subtract).then_inc(wx_lo_ready, 1)
                if ahead:
                    dve.wait_ge(ln_aggr, SC * graphs(p + 1, m))
                    ln_eps(m)
                    dve.wait_ge(adj_loaded[m], loads(p + 1))
                    make_mask(m)
                    dve.wait_ge(ln_rstd_ready, graphs(p + 1, m))
                    ln_scale(m)
                pre_n(p, q, 1)
                if ahead:
                    dve.wait_ge(ln_rs_ready, graphs(p + 1, m))
                    ln_center(m)
                update(p, q, 1)
                if l < LAYERS - 1:
                    update_lo(p, q, 1)
                if ahead:
                    dve.wait_ge(ln_hi_ready, graphs(p + 1, m))
                    ln_lo(m)

            def pair(p, first=False, last=False):
                for q in range(ITEMS):
                    item(p, q, first, last)

            def first_ln(m):
                dve.wait_ge(x_loaded[m], 16)
                ln_statistics(m)
                dve.wait_ge(ln_stats, SC * (m + 1))
                ln_mean_var(m)
                dve.wait_ge(ln_aggr, SC * (m + 1))
                ln_eps(m)

            for g in range(2):
                dve.wait_ge(wih_loaded[g], 16)
            dve.tensor_reduce(wmax[:, 1:2], wih_sb[:, :, :].rearrange("p a b -> p (a b)"), AX.X, ALU.max,
                              apply_absolute_value=True).then_inc(wmax_ready, 1)
            dve.wait_ge(w0_loaded, 16)
            dve.wait_ge(w_loaded, 16 * (LAYERS - 1))
            dve.tensor_reduce(wmax[:, 0:1], w_sb[:, :, :, :].rearrange("p a b c -> p (a b c)"), AX.X, ALU.max,
                              apply_absolute_value=True).then_inc(wmax_ready, 1)
            dve.wait_ge(whh_loaded, 16)
            dve.tensor_reduce(wmax[:, 2:3], whh_sb[:, :, :].rearrange("p a b -> p (a b)"), AX.X, ALU.max,
                              apply_absolute_value=True).then_inc(wmax_ready, 1)
            first_ln(0)
            dve.wait_ge(wmax_all_ready, 1)
            dve.scalar_tensor_tensor(out=bound[:, 0:1], in0=wmax_all[:, 0:1], scalar=D / AGG_SCALE,
                                     in1=wmax_all[:, 1:2], op0=ALU.mult, op1=ALU.mult).then_inc(scale_step, 1)
            dve.wait_ge(scale_step, 1)
            dve.scalar_tensor_tensor(out=bound[:, 1:2], in0=wmax_all[:, 2:3], scalar=1.0 / H_SCALE,
                                     in1=bound[:, 0:1], op0=ALU.mult, op1=ALU.max).then_inc(scale_step, 1)
            dve.wait_ge(scale_step, 2)
            dve.tensor_scalar(bound[:, 0:1], bound[:, 1:2], 1e-30, None, ALU.max).then_inc(scale_step, 1)
            dve.wait_ge(scale_step, 3)
            dve.tensor_scalar(pow2[:, :].bitcast(I32), bound[:, 0:1].bitcast(I32), POW2_BITS, None,
                              ALU.bitwise_and).then_inc(scale_step, 1)
            dve.wait_ge(scale_step, 4)
            dve.reciprocal(rpow2[:, :], pow2[:, :]).then_inc(scale_step, 1)
            dve.wait_ge(scale_step, 5)
            dve.tensor_scalar(wx_scale[:, :], rpow2[:, :], 2.0 ** 14 / AGG_SCALE, None,
                              ALU.mult).then_inc(scales_ready, 1)
            dve.tensor_scalar(wh_scale[:, :], rpow2[:, :], 2.0 ** 14 / H_SCALE, None,
                              ALU.mult).then_inc(scales_ready, 1)
            dve.tensor_scalar(gate_scale[:, :], rpow2[:, :], 2.0 ** 14, None, ALU.mult).then_inc(scales_ready, 1)
            dve.tensor_scalar(gate_unscale[:, :], pow2[:, :], 2.0 ** -14, None, ALU.mult).then_inc(scales_ready, 1)
            dve.wait_ge(b_loaded, 32)
            dve.tensor_tensor(bsum[:, :], bih_sb[:, :], bhh_sb[:, :], ALU.add).then_inc(biases_ready, 1)
            dve.wait_ge(scales_ready, 4)
            dve.tensor_scalar(bhn[:, :], bhh_sb[:, 2 * DC:3 * DC], gate_scale[:, 0:1], None,
                              ALU.mult).then_inc(biases_ready, 1)
            dve.wait_ge(ln_rstd_ready, 1)
            ln_scale(0)
            dve.wait_ge(ln_rs_ready, 1)
            ln_center(0)
            for n in range(PER_LAYER):
                l, c, cols = product(n)
                dve.wait_ge(wx_hi_ready, n + 1)
                dve.scalar_tensor_tensor(out=wx_lo[:, l, c, cols], in0=product_bank(n), scalar=wx_scale[:, 0:1],
                                         in1=wx_hi[:, l, c, cols], op0=ALU.mult,
                                         op1=ALU.subtract).then_inc(wx_lo_ready, 1)
            dve.wait_ge(ln_hi_ready, 1)
            ln_lo(0)
            dve.wait_ge(adj_loaded[0], 16)
            make_mask(0)
            first_ln(1)
            copy_turned_lo(0, 0)
            dve.wait_ge(ln_rstd_ready, 2)
            ln_scale(1)
            dve.wait_ge(ln_rs_ready, 2)
            ln_center(1)
            dve.wait_ge(biases_ready, 2)
            pair(0, first=True)
            with pairs_between(mybir.EngineType.DVE) as p:
                pair(p)
            pair(PAIRS - 1, last=True)
            for m in range(2):
                add_out(PAIRS - 1, m)

        @block.tensor
        def _(pe):
            def turn(p, q):
                l, m = q % ITEMS // 2, q % 2
                for i, (nat, tr, done) in enumerate(((nat_hi[m], hT_hi[m][l % 2], turned_hi),
                                                     (nat_lo[m], hT_lo[m][l % 2], turned_lo))):
                    for c in range(SC):
                        for d in range(DC):
                            if l == 0:
                                at, src = d * N + c * P, nat[:, c, d * P:(d + 1) * P]
                            else:
                                at, src = c * D + d * P, tr[:, d, c * P:(c + 1) * P]
                            last = pe.transpose(turn_h[i][:, at:at + P], src, ident_h[:, :])
                    last.then_inc(done, 1)

            def turn_out(m):
                for i in range(2):
                    for c in range(SC // 2):
                        for d in range(DC):
                            at = c * D + d * P
                            t0 = (i * SC // 2 + c) * P
                            last = pe.transpose(turn_ps[i][:, at:at + P], hT[m][:, d, t0:t0 + P], ident_f[:, :])
                    last.then_inc(out_turned, 1)

            def hidden(dst, l, m, g, stop):
                hi, lo = hT_hi[m][l % 2], hT_lo[m][l % 2]
                cols = slice(g * P, (g + 1) * P)
                for d in range(DC):
                    pe.matmul(dst[:, :], wh_hi[:, d, cols], hi[:, d, :], start=d == 0, stop=False)
                    pe.matmul(dst[:, :], wh_hi[:, d, cols], lo[:, d, :], start=False, stop=False)
                    last = pe.matmul(dst[:, :], wh_lo[:, d, cols], hi[:, d, :], start=False,
                                     stop=stop and d == DC - 1)
                return last

            def incoming(dst, l, g, start):
                cols = slice(g * P, (g + 1) * P)
                for d in range(DC):
                    pe.matmul(dst[:, :], wx_hi[:, l, d, cols], agg_hi[:, d, :], start=start and d == 0, stop=False)
                    pe.matmul(dst[:, :], wx_lo[:, l, d, cols], agg_hi[:, d, :], start=False, stop=False)
                    last = pe.matmul(dst[:, :], wx_hi[:, l, d, cols], agg_lo[:, d, :], start=False,
                                     stop=d == DC - 1)
                return last

            def item(p, q, first, last):
                l, m = q // 2, q % 2
                before = not (first and q == 0)
                if q < 2 and not first:
                    pe.wait_ge(turned_hi_copied, items(p, q))
                    pe.wait_ge(turned_lo_copied, items(p, q))
                    pe.wait_ge(h_new, halves(p - 1, ITEMS - 2 + m, DC - 1))
                    turn_out(m)
                if l == 0:
                    pe.wait_ge(mask_ready, graphs(p, m))
                else:
                    pe.wait_ge(turned_hi_copied, items(p, q))
                    pe.wait_ge(turned_lo_copied, items(p, q))
                for j in range(DC):
                    cols = slice(j * P, (j + 1) * P)
                    for c in range(SC):
                        pe.matmul(agg_ps[j][:, :], nat_hi[m][:, c, cols], mask[m][:, c, :],
                                  start=c == 0, stop=False)
                        mm = pe.matmul(agg_ps[j][:, :], nat_lo[m][:, c, cols], mask[m][:, c, :],
                                       start=False, stop=c == SC - 1)
                    mm.then_inc(agg_ready, 1)
                if l == 0:
                    pe.wait_ge(turned_hi_copied, items(p, q))
                    pe.wait_ge(turned_lo_copied, items(p, q))
                if not before:
                    pe.wait_ge(wh_lo_ready, 1)
                    pe.wait_ge(wx_lo_ready, PER_LAYER)
                if first and q == 2 * l and l > 0:
                    pe.wait_ge(wx_lo_ready, PER_LAYER + l)
                if before:
                    pe.wait_ge(pre_ready, halves(p, q - 1, DC - 1))
                hidden(hn_ps, l, m, 2 * DC, True).then_inc(hn_ready, 1)
                hidden(r_ps, l, m, 0, False)
                if before:
                    pe.wait_ge(z_sig, halves(p, q - 1, DC - 1))
                hidden(z_ps, l, m, DC, False)
                pe.wait_ge(agg_hi_ready, halves(p, q, DC - 1))
                pe.wait_ge(agg_lo_ready, halves(p, q, DC - 1))
                incoming(r_ps, l, 0, False).then_inc(r_ready, 1)
                incoming(in_ps, l, 2 * DC, True).then_inc(in_ready, 1)
                incoming(z_ps, l, DC, False).then_inc(z_ready, 1)
                if q < ITEMS - 1 or not last:
                    nl = (q + 1) % ITEMS // 2
                    nm = (q + 1) % 2
                    if nl == 0:
                        pe.wait_ge(ln_hi_ready, graphs(p + (q + 1) // ITEMS, nm))
                        pe.wait_ge(ln_lo_ready, graphs(p + (q + 1) // ITEMS, nm))
                    else:
                        pe.wait_ge(h_hi_ready, splits(p, q - 1, DC - 1))
                        pe.wait_ge(h_lo_ready, splits(p, q - 1, DC - 1))
                    if q < 2 and not first:
                        pe.wait_ge(out_added, 2 * graphs(p - 1, m))
                    turn(p, q + 1)
                pe.wait_ge(r_sig, halves(p, q, 0))
                hidden(r_ps, l, m, 1, False)
                incoming(r_ps, l, 1, False).then_inc(r_ready, 1)
                pe.wait_ge(gated, halves(p, q, 0))
                hidden(hn_ps, l, m, 2 * DC + 1, True).then_inc(hn_ready, 1)
                pe.wait_ge(pre_ready, halves(p, q, 0))
                incoming(in_ps, l, 2 * DC + 1, True).then_inc(in_ready, 1)
                pe.wait_ge(z_sig, halves(p, q, 0))
                hidden(z_ps, l, m, DC + 1, False)
                incoming(z_ps, l, DC + 1, False).then_inc(z_ready, 1)

            def pair(p, first=False, last=False):
                for q in range(ITEMS):
                    item(p, q, first, last)

            pe.wait_ge(consts_ready, 2)
            for _ in range(WARM_UP):
                pe.matmul(hn_ps[:, 0:P], ident_h[:, :], ident_h[:, :], start=True, stop=True)
            pe.wait_ge(w0_loaded, 16)
            for n in range(WPRODS):
                l, c, cols = product(n)
                if n < 2:
                    pe.wait_ge(wih_loaded[n], 16)
                if n == PER_LAYER:
                    pe.wait_ge(w_loaded, 16 * (LAYERS - 1))
                if n >= 2 * PER_LAYER:
                    pe.wait_ge(prod_copied, n + 1 - 2 * PER_LAYER)
                for e in range(DC):
                    mm = pe.matmul(product_bank(n), w_sb[:, l, e, c * P:(c + 1) * P], wih_sb[:, e, cols],
                                   start=e == 0, stop=e == DC - 1)
                mm.then_inc(prod_ready, 1)
            pe.wait_ge(ln_hi_ready, 1)
            pe.wait_ge(ln_lo_ready, 1)
            pe.wait_ge(prod_copied, WPRODS - PER_LAYER)
            turn(0, 0)
            pair(0, first=True)
            with pairs_between(mybir.EngineType.PE) as p:
                pair(p)
            pair(PAIRS - 1, last=True)
            pe.wait_ge(h_new, halves(PAIRS - 1, ITEMS - 2, DC - 1))
            turn_out(0)
            pe.wait_ge(h_new, halves(PAIRS - 1, ITEMS - 1, DC - 1))
            pe.wait_ge(out_added, 2 * graphs(PAIRS - 1, 0))
            turn_out(1)


def kernel(x, adj, L0_gnn_weight, L0_gnn_w_ih, L0_gnn_w_hh, L0_gnn_b_ih, L0_gnn_b_hh):
    import numpy as np
    import concourse.bacc as bacc
    from concourse.bass_utils import run_bass_kernel_spmd

    arrays = {
        "x": np.ascontiguousarray(x),
        "adj": np.ascontiguousarray(adj),
        "w_t": np.ascontiguousarray(np.transpose(L0_gnn_weight, (0, 2, 1))),
        "wih_t": np.ascontiguousarray(np.transpose(L0_gnn_w_ih)),
        "whh_t": np.ascontiguousarray(np.transpose(L0_gnn_w_hh)),
        "bih": np.ascontiguousarray(np.transpose(np.reshape(L0_gnn_b_ih, (-1, P)))),
        "bhh": np.ascontiguousarray(np.transpose(np.reshape(L0_gnn_b_hh, (-1, P)))),
    }
    nc = bacc.Bacc("TRN2", target_bir_lowering=False, num_devices=1)
    args = [nc.dram_tensor(k, a.shape, mybir.dt.from_np(a.dtype), kind="ExternalInput").ap()
            for k, a in arrays.items()]
    args.append(nc.dram_tensor("out", x.shape, F32, kind="ExternalOutput").ap())
    gnn_kernel(nc, *args)
    r = run_bass_kernel_spmd(nc, [arrays], core_ids=[0])
    return r.results[0]["out"]
```
